# Optimizing a Trainium2 kernel written in Bass

```python
import numpy as np
import jax
import jax.numpy as jnp

def _softmax(x, axis=-1):
    return jax.nn.softmax(x, axis=axis)

def _gelu(x):
    return jax.nn.gelu(x, approximate=True)

def _silu(x):
    return jax.nn.silu(x)

def _sigmoid(x):
    return jax.nn.sigmoid(x)

def _layernorm(x, axis=-1, eps=1e-05):
    m = jnp.mean(x, axis=axis, keepdims=True)
    v = jnp.var(x, axis=axis, keepdims=True)
    return (x - m) / jnp.sqrt(v + eps)

def _scatter_add(tgt, idx, src, axis=0):
    return tgt.at[idx].add(src)

def _segment_sum(src, seg, n):
    return jax.ops.segment_sum(src, seg, n)
kernel_name = 'mk_dlrm_tower_d1_rec_r8_52bc2c'

def setup_inputs(seed: int=0):
    np.random.seed(seed)
    _w = jnp.asarray

    def _rec_inputs():
        import jax
        import jax.numpy as jnp
        _tk = jax.random.key(seed)
        dense_ctx = jax.random.normal(jax.random.fold_in(_tk, 190), (2048, 16), jnp.float32)
        ids = jnp.stack([jax.random.randint(jax.random.fold_in(_tk, 200 + f), (2048,), 0, v, jnp.int32) for f, v in enumerate([1250, 1000, 125000, 1000, 125000, 1250, 12500, 125000, 1000, 1250, 1250, 12500, 12500, 1000, 1250, 12500, 12500, 1000, 1000, 12500, 12500, 1000, 12500, 1000, 1250, 1000, 1250, 1250, 1000, 1250, 1000, 1000])], axis=1)
        tbl_0 = 0.05 * jax.random.normal(jax.random.fold_in(_tk, 500 + 0), (1250, 64), jnp.float32)
        tbl_1 = 0.05 * jax.random.normal(jax.random.fold_in(_tk, 500 + 1), (1000, 64), jnp.float32)
        tbl_2 = 0.05 * jax.random.normal(jax.random.fold_in(_tk, 500 + 2), (125000, 64), jnp.float32)
        tbl_3 = 0.05 * jax.random.normal(jax.random.fold_in(_tk, 500 + 3), (1000, 64), jnp.float32)
        tbl_4 = 0.05 * jax.random.normal(jax.random.fold_in(_tk, 500 + 4), (125000, 64), jnp.float32)
        tbl_5 = 0.05 * jax.random.normal(jax.random.fold_in(_tk, 500 + 5), (1250, 64), jnp.float32)
        tbl_6 = 0.05 * jax.random.normal(jax.random.fold_in(_tk, 500 + 6), (12500, 64), jnp.float32)
        tbl_7 = 0.05 * jax.random.normal(jax.random.fold_in(_tk, 500 + 7), (125000, 64), jnp.float32)
        tbl_8 = 0.05 * jax.random.normal(jax.random.fold_in(_tk, 500 + 8), (1000, 64), jnp.float32)
        tbl_9 = 0.05 * jax.random.normal(jax.random.fold_in(_tk, 500 + 9), (1250, 64), jnp.float32)
        tbl_10 = 0.05 * jax.random.normal(jax.random.fold_in(_tk, 500 + 10), (1250, 64), jnp.float32)
        tbl_11 = 0.05 * jax.random.normal(jax.random.fold_in(_tk, 500 + 11), (12500, 64), jnp.float32)
        tbl_12 = 0.05 * jax.random.normal(jax.random.fold_in(_tk, 500 + 12), (12500, 64), jnp.float32)
        tbl_13 = 0.05 * jax.random.normal(jax.random.fold_in(_tk, 500 + 13), (1000, 64), jnp.float32)
        tbl_14 = 0.05 * jax.random.normal(jax.random.fold_in(_tk, 500 + 14), (1250, 64), jnp.float32)
        tbl_15 = 0.05 * jax.random.normal(jax.random.fold_in(_tk, 500 + 15), (12500, 64), jnp.float32)
        tbl_16 = 0.05 * jax.random.normal(jax.random.fold_in(_tk, 500 + 16), (12500, 64), jnp.float32)
        tbl_17 = 0.05 * jax.random.normal(jax.random.fold_in(_tk, 500 + 17), (1000, 64), jnp.float32)
        tbl_18 = 0.05 * jax.random.normal(jax.random.fold_in(_tk, 500 + 18), (1000, 64), jnp.float32)
        tbl_19 = 0.05 * jax.random.normal(jax.random.fold_in(_tk, 500 + 19), (12500, 64), jnp.float32)
        tbl_20 = 0.05 * jax.random.normal(jax.random.fold_in(_tk, 500 + 20), (12500, 64), jnp.float32)
        tbl_21 = 0.05 * jax.random.normal(jax.random.fold_in(_tk, 500 + 21), (1000, 64), jnp.float32)
        tbl_22 = 0.05 * jax.random.normal(jax.random.fold_in(_tk, 500 + 22), (12500, 64), jnp.float32)
        tbl_23 = 0.05 * jax.random.normal(jax.random.fold_in(_tk, 500 + 23), (1000, 64), jnp.float32)
        tbl_24 = 0.05 * jax.random.normal(jax.random.fold_in(_tk, 500 + 24), (1250, 64), jnp.float32)
        tbl_25 = 0.05 * jax.random.normal(jax.random.fold_in(_tk, 500 + 25), (1000, 64), jnp.float32)
        tbl_26 = 0.05 * jax.random.normal(jax.random.fold_in(_tk, 500 + 26), (1250, 64), jnp.float32)
        tbl_27 = 0.05 * jax.random.normal(jax.random.fold_in(_tk, 500 + 27), (1250, 64), jnp.float32)
        tbl_28 = 0.05 * jax.random.normal(jax.random.fold_in(_tk, 500 + 28), (1000, 64), jnp.float32)
        tbl_29 = 0.05 * jax.random.normal(jax.random.fold_in(_tk, 500 + 29), (1250, 64), jnp.float32)
        tbl_30 = 0.05 * jax.random.normal(jax.random.fold_in(_tk, 500 + 30), (1000, 64), jnp.float32)
        tbl_31 = 0.05 * jax.random.normal(jax.random.fold_in(_tk, 500 + 31), (1000, 64), jnp.float32)
        _rk = jax.random.fold_in(_tk, 7)
        W_top1 = 0.0428746 * jax.random.normal(jax.random.fold_in(_tk, 801), (544, 512), jnp.float32)
        W_top2 = 0.0441942 * jax.random.normal(jax.random.fold_in(_tk, 802), (512, 256), jnp.float32)
        W_top3 = 0.0625 * jax.random.normal(jax.random.fold_in(_tk, 803), (256, 1), jnp.float32)
        b_top1 = jnp.zeros((512,), jnp.float32)
        b_top2 = jnp.zeros((256,), jnp.float32)
        return (dense_ctx, ids, tbl_0, tbl_1, tbl_2, tbl_3, tbl_4, tbl_5, tbl_6, tbl_7, tbl_8, tbl_9, tbl_10, tbl_11, tbl_12, tbl_13, tbl_14, tbl_15, tbl_16, tbl_17, tbl_18, tbl_19, tbl_20, tbl_21, tbl_22, tbl_23, tbl_24, tbl_25, tbl_26, tbl_27, tbl_28, tbl_29, tbl_30, tbl_31, W_top1, b_top1, W_top2, b_top2, W_top3)
    dense_ctx, ids, tbl_0, tbl_1, tbl_2, tbl_3, tbl_4, tbl_5, tbl_6, tbl_7, tbl_8, tbl_9, tbl_10, tbl_11, tbl_12, tbl_13, tbl_14, tbl_15, tbl_16, tbl_17, tbl_18, tbl_19, tbl_20, tbl_21, tbl_22, tbl_23, tbl_24, tbl_25, tbl_26, tbl_27, tbl_28, tbl_29, tbl_30, tbl_31, W_top1, b_top1, W_top2, b_top2, W_top3 = _rec_inputs()

    def _L0_rec_setup():
        import jax, jax.numpy as jnp
        import numpy as np
        B, F, D = (512, 32, 64)
        II, JJ = np.triu_indices(F, k=1)
        P = II.shape[0]
        key = jax.random.key(seed)
        kx, kk = jax.random.split(key)
        x = jax.random.normal(kx, (B, F, D), dtype=jnp.float32)
        kernels = jax.random.normal(kk, (P, D, D), dtype=jnp.float32) * 0.001
        return {'x': x, 'kernels': kernels}
    _L0_rec_all = _L0_rec_setup()
    _L0_rec_in = {k: v for k, v in _L0_rec_all.items() if k in ('kernels',)}
    del _L0_rec_all
    return {'dense_ctx': dense_ctx, 'ids': ids, 'tbl_0': tbl_0, 'tbl_1': tbl_1, 'tbl_2': tbl_2, 'tbl_3': tbl_3, 'tbl_4': tbl_4, 'tbl_5': tbl_5, 'tbl_6': tbl_6, 'tbl_7': tbl_7, 'tbl_8': tbl_8, 'tbl_9': tbl_9, 'tbl_10': tbl_10, 'tbl_11': tbl_11, 'tbl_12': tbl_12, 'tbl_13': tbl_13, 'tbl_14': tbl_14, 'tbl_15': tbl_15, 'tbl_16': tbl_16, 'tbl_17': tbl_17, 'tbl_18': tbl_18, 'tbl_19': tbl_19, 'tbl_20': tbl_20, 'tbl_21': tbl_21, 'tbl_22': tbl_22, 'tbl_23': tbl_23, 'tbl_24': tbl_24, 'tbl_25': tbl_25, 'tbl_26': tbl_26, 'tbl_27': tbl_27, 'tbl_28': tbl_28, 'tbl_29': tbl_29, 'tbl_30': tbl_30, 'tbl_31': tbl_31, 'W_top1': W_top1, 'b_top1': b_top1, 'W_top2': W_top2, 'b_top2': b_top2, 'W_top3': W_top3, 'L0_rec_kernels': _L0_rec_in['kernels']}

def reference(dense_ctx, ids, tbl_0, tbl_1, tbl_2, tbl_3, tbl_4, tbl_5, tbl_6, tbl_7, tbl_8, tbl_9, tbl_10, tbl_11, tbl_12, tbl_13, tbl_14, tbl_15, tbl_16, tbl_17, tbl_18, tbl_19, tbl_20, tbl_21, tbl_22, tbl_23, tbl_24, tbl_25, tbl_26, tbl_27, tbl_28, tbl_29, tbl_30, tbl_31, W_top1, b_top1, W_top2, b_top2, W_top3, L0_rec_kernels):
    import jax
    import jax.numpy as jnp

    def _L0_rec_ref(x, kernels):
        import jax, jax.numpy as jnp
        import numpy as np
        B, F, D = (512, 32, 64)
        II, JJ = np.triu_indices(F, k=1)
        P = II.shape[0]
        z = jnp.sum(x, axis=-1)
        xi = x[:, II, :]
        xj = x[:, JJ, :]
        outer = jnp.einsum('bpd,pde,bpe->bp', xi, kernels, xj)
        return jnp.concatenate([z, outer], axis=1)
    e = jnp.stack([tbl_0[ids[:, 0]], tbl_1[ids[:, 1]], tbl_2[ids[:, 2]], tbl_3[ids[:, 3]], tbl_4[ids[:, 4]], tbl_5[ids[:, 5]], tbl_6[ids[:, 6]], tbl_7[ids[:, 7]], tbl_8[ids[:, 8]], tbl_9[ids[:, 9]], tbl_10[ids[:, 10]], tbl_11[ids[:, 11]], tbl_12[ids[:, 12]], tbl_13[ids[:, 13]], tbl_14[ids[:, 14]], tbl_15[ids[:, 15]], tbl_16[ids[:, 16]], tbl_17[ids[:, 17]], tbl_18[ids[:, 18]], tbl_19[ids[:, 19]], tbl_20[ids[:, 20]], tbl_21[ids[:, 21]], tbl_22[ids[:, 22]], tbl_23[ids[:, 23]], tbl_24[ids[:, 24]], tbl_25[ids[:, 25]], tbl_26[ids[:, 26]], tbl_27[ids[:, 27]], tbl_28[ids[:, 28]], tbl_29[ids[:, 29]], tbl_30[ids[:, 30]], tbl_31[ids[:, 31]]], axis=1)
    z = _L0_rec_ref(e, L0_rec_kernels)
    z = z.reshape(z.shape[0], -1)
    h = jnp.concatenate([z, dense_ctx], axis=1)
    h = jnp.maximum(h @ W_top1 + b_top1, 0.0)
    h = jnp.maximum(h @ W_top2 + b_top2, 0.0)
    y = h @ W_top3
    return y

_drawn_inputs = setup_inputs


def setup_inputs(seed=0):
    import zlib

    import numpy as np

    out = dict(_drawn_inputs(seed))
    spreads = {'b_top1': (0.0, 0.1), 'b_top2': (0.0, 0.1)}
    factors = {'L0_rec_kernels': 64.0}
    for name, (base, spread) in spreads.items():
        noise = np.random.default_rng([zlib.crc32(name.encode()), seed]).standard_normal(out[name].shape)
        drawn = base * np.exp(spread * noise) if base else spread * noise
        out[name] = jnp.asarray(drawn.astype(out[name].dtype))
    for name, factor in factors.items():
        out[name] = (out[name] * factor).astype(out[name].dtype)
    return out
```

```python
from contextlib import ExitStack

import concourse.bass as bass
from concourse import mybir

ALU = mybir.AluOpType
ACT = mybir.ActivationFunctionType
F32 = mybir.dt.float32
F32R = mybir.dt.float32r
I32 = mybir.dt.int32

P = 128
FEATURES = 32
D = 64
BATCH = 2048
DENSE = 16
H1 = 512
H2 = 256
CHUNK = 512
CHUNKS = BATCH // CHUNK
TILES = CHUNK // P
ROWS = FEATURES // 2

UNITS = [(m, a) for m in range(ROWS) for a in range(m + 1)]
NU = len(UNITS)
NB = NU // 2
LEFT = FEATURES - 1
KGROUPS = sum(2 * m + 1 for m in range(ROWS))
KBLOCK = 4
KBLOCKS = KGROUPS // KBLOCK
KCOLS = KBLOCK * P
KSLOTS = 4
GSLOTS = 4
XSLOTS = 4
TSLOTS = 3
PSLOTS = 4
AHEAD = 2
ZGROUPS = 64
ZBANKS = -(-2 * NU // ZGROUPS)
Z_LAST_ROWS = 2 * (2 * NU % ZGROUPS) // 4
PAIR_PAD = 32


def unit_at(m, a):
    return m * (m + 1) // 2 + a


def k_groups(u):
    m, a = UNITS[u]
    return [m * m + 2 * a] if a == m else [m * m + 2 * a, m * m + 2 * a + 1]


K_LAST_UNIT = [next(u for u in range(NU) if KBLOCK * b + KBLOCK - 1 in k_groups(u)) for b in range(KBLOCKS)]


TURN_AT = {unit_at(m, 0): m + AHEAD for m in range(ROWS - AHEAD)}
K_SPLIT_AT = {}
for _b in range(KSLOTS, KBLOCKS):
    K_SPLIT_AT.setdefault(K_LAST_UNIT[_b - KSLOTS] + 1, []).append(_b)


def wait(eng, sem, c, per_chunk, n):
    if isinstance(c, int) and c * per_chunk + n <= 0:
        return
    eng.wait_ge(sem, c * per_chunk + n)


def program(nc, ids, dense, tables, kg, w1, w2, columns, y):
    ctx = ExitStack()
    with ctx:
        def sb(name, shape, dt=F32):
            return ctx.enter_context(nc.sbuf_tensor(name, shape, dt))

        def sem(name):
            return ctx.enter_context(nc.semaphore(name))

        x_hi = sb("x_hi", [P, LEFT, CHUNK], F32R)
        x_lo = sb("x_lo", [P, LEFT, CHUNK], F32R)
        x_pair = sb("x_pair", [P, XSLOTS, CHUNK])
        x_rows = sb("x_rows", [P, GSLOTS, TILES, 2 * D])
        k_ring = sb("k_ring", [P, KSLOTS, KCOLS], F32R)
        product = sb("product", [P, PSLOTS, 2, CHUNK])
        w1_sb = sb("w1_sb", [P, ZBANKS, H1])
        w2_sb = sb("w2_sb", [P, H1 // P, H2])
        columns_sb = sb("columns_sb", [P, H1 // P + 2 * (H2 // P)])
        b1_sb, b2_sb, w3_sb = columns_sb[:, 0:4], columns_sb[:, 4:6], columns_sb[:, 6:8]
        z_sb = sb("z_sb", [P, ZBANKS, CHUNK])
        h1_sb = sb("h1_sb", [P, H1 // P, CHUNK])
        h2_sb = sb("h2_sb", [P, H2 // P, CHUNK])
        ident = sb("ident", [P, P])
        selector = sb("selector", [P, 62])
        ids_sb = sb("ids_sb", [P, FEATURES * TILES], I32)
        dense_sb = sb("dense_sb", [P, TILES, PAIR_PAD])
        k_raw = h1_sb
        y_sb = h1_sb[0:1, 0, :]

        ps_t = ctx.enter_context(nc.psum_tensor("ps_t", [P, 2 * TSLOTS, CHUNK], F32))
        ps_z = ctx.enter_context(nc.psum_tensor("ps_z", [P, CHUNK], F32))
        ps_x = ctx.enter_context(nc.psum_tensor("ps_x", [P, CHUNK], F32))
        k_store = nc.dram_tensor("k_store", (P, KGROUPS * P), F32, kind="Internal").ap()

        weights_in = sem("weights_in")
        ones_set = sem("ones_set")
        consts_set = sem("consts_set")
        selector_set = sem("selector_set")
        ids_in = sem("ids_in")
        dense_in = sem("dense_in")
        gathered = [sem(f"gathered{s}") for s in range(GSLOTS)]
        may_gather = sem("may_gather")
        turned = sem("turned")
        hi_ready = sem("hi_ready")
        lo_ready = sem("lo_ready")
        x_ready = sem("x_ready")
        pair_ready = sem("pair_ready")
        k_raw_in = [sem(f"k_raw_in{s}") for s in range(KSLOTS)]
        k_hi_ready = sem("k_hi_ready")
        k_split = sem("k_split")
        k_stored = [sem(f"k_stored{s}") for s in range(KSLOTS)]
        k_loaded = [sem(f"k_loaded{s}") for s in range(KSLOTS)]
        t_ready = sem("t_ready")
        product_ready = sem("product_ready")
        sums_done = sem("sums_done")
        dense_free = sem("dense_free")
        z_copied = sem("z_copied")
        h1_summed = sem("h1_summed")
        h1_ready = sem("h1_ready")
        h2_summed = sem("h2_summed")
        h2_ready = sem("h2_ready")
        y_summed = sem("y_summed")
        y_ready = sem("y_ready")
        y_stored = sem("y_stored")
        WEIGHTS = 3 * 16

        block = ctx.enter_context(nc.Block())

        @block.sync
        def _(sp):
            for b in range(KBLOCKS + 2):
                if b < KBLOCKS:
                    if b >= KSLOTS:
                        sp.wait_ge(k_split, b - KSLOTS + 1)
                    for half in range(2):
                        sp.dma_start(k_raw[half * D:half * D + D, b % KSLOTS, :],
                                     kg[:, b * KCOLS:(b + 1) * KCOLS]).then_inc(k_raw_in[b % KSLOTS], 16)
                if b == 1:
                    sp.dma_start(w1_sb[:], w1.rearrange("(k p) n -> p k n", p=P)).then_inc(weights_in, 16)
                    sp.dma_start(w2_sb[:], w2.rearrange("(k p) n -> p k n", p=P)).then_inc(weights_in, 16)
                    sp.dma_start(columns_sb[:], columns).then_inc(weights_in, 16)
                if b >= 2:
                    o = b - 2
                    sp.wait_ge(k_split, o + 1)
                    sp.dma_start(k_store[:, o * KCOLS:(o + 1) * KCOLS],
                                 k_ring[:, o % KSLOTS, :].bitcast(F32)).then_inc(k_stored[o % KSLOTS], 16)
            for s in range(KSLOTS):
                sp.wait_ge(k_stored[s], 16 * (KBLOCKS // KSLOTS))
            with sp.Fori(1, CHUNKS) as c:
                for b in range(KBLOCKS):
                    if b < KSLOTS:
                        wait(sp, t_ready, c - 1, NU, K_LAST_UNIT[KBLOCKS + b - KSLOTS] + 1)
                    else:
                        wait(sp, t_ready, c, NU, K_LAST_UNIT[b - KSLOTS] + 1)
                    sp.dma_start(k_ring[:, b % KSLOTS, :].bitcast(F32),
                                 k_store[:, b * KCOLS:(b + 1) * KCOLS]).then_inc(k_loaded[b % KSLOTS], 16)

        @block.gpsimd
        def _(pool):
            nc.gpsimd.memset(ident[:], 1.0).then_inc(ones_set, 1)
            pool.wait_ge(ones_set, 1)
            nc.gpsimd.affine_select(out=ident[:], in_=ident[:], compare_op=ALU.is_equal, fill=0.0, base=0,
                                    pattern=[[-1, P]], channel_multiplier=1).then_inc(consts_set, 1)
            pool.wait_ge(consts_set, 1)
            with pool.Fori(0, CHUNKS) as c:
                pool.dma_start(ids_sb[:], ids[bass.ds(c * P, P), :]).then_inc(ids_in, 16)
                pool.wait_ge(ids_in, c * 16 + 16)
                pool.sem_inc(may_gather, 1)
                for m in range(ROWS):
                    if m >= GSLOTS:
                        pool.wait_ge(turned, c * ROWS + m - GSLOTS + 1)
                        pool.sem_inc(may_gather, 1)
                    for f in (2 * m, 2 * m + 1):
                        for t in range(TILES):
                            n = f * TILES + t
                            at = (f % 2) * D
                            nc.gpsimd.indirect_dma_start(
                                x_rows[:, m % GSLOTS, t, at:at + D], None, tables[f],
                                bass.IndirectOffsetOnAxis(ap=ids_sb[:, n:n + 1], axis=0),
                            ).then_inc(gathered[m % GSLOTS], 16)
                pool.wait_ge(dense_free, c + 1)
                pool.dma_start(dense_sb[:, :, Z_LAST_ROWS:Z_LAST_ROWS + DENSE],
                               dense[bass.ds(c * P, P), :].rearrange("p (t k) -> p t k", k=DENSE),
                               ).then_inc(dense_in, 16)
                pool.wait_ge(turned, c * ROWS + ROWS)

        def chunk_tensor(pe, c, first):
            def turn(m):
                uses = ROWS // GSLOTS
                wait(pe, gathered[m % GSLOTS], c, 32 * TILES * uses, 32 * TILES * (m // GSLOTS + 1))
                wait(pe, pair_ready, c, ROWS, m)
                for t in range(TILES):
                    ins = pe.transpose(ps_x[:, t * P:(t + 1) * P], x_rows[:, m % GSLOTS, t, :], ident[:])
                ins.then_inc(turned, 1)

            def stage1(u):
                m, a = UNITS[u]
                if u >= TSLOTS:
                    wait(pe, product_ready, c, NU, u - TSLOTS + 1)
                elif u == 0 and not first:
                    wait(pe, product_ready, c, NU, 0)
                    wait(pe, h1_ready, c, H1 // P, 0)
                    wait(pe, h2_ready, c, H2 // P, 0)
                if a == m:
                    wait(pe, x_ready, c, LEFT, 2 * m + 1)
                elif a == m - 1:
                    wait(pe, x_ready, c, LEFT, 2 * m)
                for g, k in enumerate(k_groups(u)):
                    b, at = divmod(k, KBLOCK)
                    if at == 0:
                        if first:
                            pe.wait_ge(k_split, b + 1)
                        else:
                            wait(pe, k_loaded[b % KSLOTS], c - 1, 16 * (KBLOCKS // KSLOTS),
                                 16 * (b // KSLOTS + 1))
                    weights = k_ring[:, b % KSLOTS, at * P:(at + 1) * P]
                    bank = ps_t[:, 2 * (u % TSLOTS) + g, :]
                    pe.matmul(bank, weights, x_hi[:, 2 * a + g, :], start=True, stop=False)
                    ins = pe.matmul(bank, weights, x_lo[:, 2 * a + g, :], start=False, stop=True)
                ins.then_inc(t_ready, 1)

            def stage2(n):
                wait(pe, product_ready, c, NU, 2 * n + 2)
                bank, at = divmod(4 * n, ZGROUPS)
                if at == 0:
                    wait(pe, z_copied, c, ZBANKS, bank)
                    if n == 0 and not first:
                        wait(pe, y_ready, c, 1, 0)
                pair = at // 4
                for k in range(4):
                    u, g = 2 * n + k // 2, k % 2
                    m, a = UNITS[u]
                    moving = x_pair[:, m % XSLOTS, :] if a == m and g == 1 else product[:, u % PSLOTS, g, :]
                    ins = pe.matmul(ps_z[32 * k:32 * k + 32, :], selector[:, 30 - 2 * pair:62 - 2 * pair],
                                    moving, start=(pair == 0),
                                    stop=(pair == ZGROUPS // 4 - 1 or (n == NB - 1 and k > 0)))
                ins.then_inc(sums_done, 1)

            def mlp():
                wait(pe, dense_in, c, 16, 16)
                for t in range(TILES):
                    ins = pe.matmul(ps_z[0:32, t * P:(t + 1) * P], dense_sb[:, t, :], ident[:],
                                    start=False, stop=(t == TILES - 1))
                ins.then_inc(dense_free, 1)
                if first:
                    pe.wait_ge(weights_in, WEIGHTS)
                wait(pe, product_ready, c, NU, NU)
                for n in range(H1 // P):
                    for k in range(ZBANKS):
                        if n == 0:
                            wait(pe, z_copied, c, ZBANKS, k + 1)
                        ins = pe.matmul(ps_t[:, n, :], w1_sb[:, k, n * P:(n + 1) * P], z_sb[:, k, :],
                                        start=(k == 0), stop=(k == ZBANKS - 1))
                    ins.then_inc(h1_summed, 1)
                for n in range(H2 // P):
                    for k in range(H1 // P):
                        wait(pe, h1_ready, c, H1 // P, k + 1)
                        ins = pe.matmul(ps_t[:, H1 // P + n, :], w2_sb[:, k, n * P:(n + 1) * P],
                                        h1_sb[:, k, :], start=(k == 0), stop=(k == H1 // P - 1))
                    ins.then_inc(h2_summed, 1)
                for k in range(H2 // P):
                    wait(pe, h2_ready, c, H2 // P, k + 1)
                    ins = pe.matmul(ps_z[0:1, :], w3_sb[:, k:k + 1], h2_sb[:, k, :],
                                    start=(k == 0), stop=(k == H2 // P - 1))
                ins.then_inc(y_summed, 1)

            for m in range(AHEAD):
                turn(m)
            for u in range(NU):
                if u in TURN_AT:
                    turn(TURN_AT[u])
                stage1(u)
                if u % 2 == 1 and u >= 3:
                    stage2((u - 3) // 2)
            stage2(NB - 1)
            mlp()

        @block.tensor
        def _(pe):
            pe.wait_ge(consts_set, 1)
            pe.wait_ge(selector_set, 3)
            chunk_tensor(pe, 0, True)
            with pe.Fori(1, CHUNKS) as c:
                chunk_tensor(pe, c, False)

        def chunk_vector(dve, c, first):
            def split_x(m):
                for f in range(2 * m, min(2 * m + 2, LEFT)):
                    lanes = slice((f % 2) * D, (f % 2) * D + D)
                    wait(dve, hi_ready, c, LEFT, f + 1)
                    dve.tensor_tensor(x_lo[lanes, f, :], x_pair[lanes, m % XSLOTS, :], x_hi[lanes, f, :],
                                      ALU.subtract).then_inc(lo_ready, 1)

            def split_k(b):
                dve.wait_ge(k_hi_ready, b + 1)
                dve.tensor_tensor(k_ring[D:P, b % KSLOTS, :], k_raw[D:P, b % KSLOTS, :],
                                  k_ring[D:P, b % KSLOTS, :], ALU.subtract).then_inc(k_split, 1)

            def multiply(u):
                m, a = UNITS[u]
                wait(dve, t_ready, c, NU, u + 1)
                if a == 0:
                    wait(dve, pair_ready, c, ROWS, m + 1)
                if u >= PSLOTS:
                    wait(dve, sums_done, c, NB, (u - PSLOTS) // 2 + 1)
                elif u == 0 and not first:
                    wait(dve, sums_done, c, NB, 0)
                slot = 2 * (u % TSLOTS)
                right = x_pair[:, m % XSLOTS, :]
                if a == m:
                    ins = dve.tensor_tensor(product[:, u % PSLOTS, 0, :], ps_t[:, slot, :], right, ALU.mult)
                else:
                    ins = dve.tensor_tensor(product[:, u % PSLOTS, :, :], ps_t[:, slot:slot + 2, :],
                                            x_pair[:, m % XSLOTS:m % XSLOTS + 1, :].to_broadcast([P, 2, CHUNK]),
                                            ALU.mult)
                ins.then_inc(product_ready, 1)

            if first:
                for b in range(KSLOTS):
                    split_k(b)
            for m in range(AHEAD):
                split_x(m)
            for u in range(NU):
                multiply(u)
                if first:
                    for b in K_SPLIT_AT.get(u, []):
                        split_k(b)
                if u in TURN_AT:
                    split_x(TURN_AT[u])

        @block.vector
        def _(dve):
            dve.memset(selector[:], 0.0).then_inc(selector_set, 1)
            dve.memset(dense_sb[:], 0.0).then_inc(dense_free, 1)
            dve.wait_ge(selector_set, 1)
            dve.memset(selector[0:D, 30:31], 1.0).then_inc(selector_set, 1)
            dve.memset(selector[D:P, 31:32], 1.0).then_inc(selector_set, 1)
            chunk_vector(dve, 0, True)
            with dve.Fori(1, CHUNKS) as c:
                chunk_vector(dve, c, False)

        def chunk_scalar(act, c, first):
            def copy_x(m):
                wait(act, turned, c, ROWS, m + 1)
                if m >= XSLOTS:
                    last = unit_at(m - XSLOTS, m - XSLOTS)
                    wait(act, product_ready, c, NU, last + 1)
                    wait(act, sums_done, c, NB, last // 2 + 1)
                elif m == 0 and not first:
                    wait(act, product_ready, c, NU, 0)
                    wait(act, sums_done, c, NB, 0)
                pair = x_pair[:, m % XSLOTS, :]
                act.copy(pair, ps_x[:]).then_inc(pair_ready, 1)
                wait(act, pair_ready, c, ROWS, m + 1)
                features = range(2 * m, min(2 * m + 2, LEFT))
                own = [slice((f % 2) * D, (f % 2) * D + D) for f in features]
                other = [slice((1 - f % 2) * D, (1 - f % 2) * D + D) for f in features]
                for f, lanes in zip(features, own):
                    act.copy(x_hi[lanes, f, :], pair[lanes, :]).then_inc(hi_ready, 1)
                for f, lanes, far in zip(features, own, other):
                    act.copy(x_hi[far, f, :], pair[lanes, :])
                for f, lanes, far in zip(features, own, other):
                    wait(act, lo_ready, c, LEFT, f + 1)
                    act.copy(x_lo[far, f, :], x_lo[lanes, f, :]).then_inc(x_ready, 1)

            def round_k(b):
                wait(act, k_raw_in[b % KSLOTS], 0, 0, 32 * (b // KSLOTS + 1))
                if b >= KSLOTS:
                    act.wait_ge(t_ready, K_LAST_UNIT[b - KSLOTS] + 1)
                    act.wait_ge(k_stored[b % KSLOTS], 16 * (b // KSLOTS))
                act.copy(k_ring[:, b % KSLOTS, :], k_raw[:, b % KSLOTS, :]).then_inc(k_hi_ready, 1)

            def copy_z(k):
                if k < ZBANKS - 1:
                    wait(act, sums_done, c, NB, (k + 1) * ZGROUPS // 4)
                else:
                    wait(act, dense_free, c, 1, 2)
                act.copy(z_sb[:, k, :], ps_z[:]).then_inc(z_copied, 1)

            if first:
                for b in range(KSLOTS):
                    round_k(b)
            for m in range(AHEAD):
                copy_x(m)
            for u in range(NU):
                if first:
                    for b in K_SPLIT_AT.get(u, []):
                        round_k(b)
                if u in TURN_AT:
                    copy_x(TURN_AT[u])
                if u % (ZGROUPS // 2) == 2 and u > ZGROUPS // 2:
                    copy_z(u // (ZGROUPS // 2) - 1)
            copy_z(ZBANKS - 1)
            if first:
                act.wait_ge(weights_in, WEIGHTS)
            else:
                wait(act, y_stored, c, 16, 0)
            for n in range(H1 // P):
                wait(act, h1_summed, c, H1 // P, n + 1)
                act.activation(h1_sb[:, n, :], ps_t[:, n, :], ACT.Relu, bias=b1_sb[:, n:n + 1]).then_inc(h1_ready, 1)
            for n in range(H2 // P):
                wait(act, h2_summed, c, H2 // P, n + 1)
                act.activation(h2_sb[:, n, :], ps_t[:, H1 // P + n, :], ACT.Relu,
                               bias=b2_sb[:, n:n + 1]).then_inc(h2_ready, 1)
            wait(act, y_summed, c, 1, 1)
            act.copy(y_sb, ps_z[0:1, :]).then_inc(y_ready, 1)
            wait(act, y_ready, c, 1, 1)
            act.dma_start(y[:, bass.ds(c * CHUNK, CHUNK)], y_sb).then_inc(y_stored, 16)

        @block.scalar
        def _(act):
            chunk_scalar(act, 0, True)
            with act.Fori(1, CHUNKS) as c:
                chunk_scalar(act, c, False)
            act.wait_ge(y_stored, 16 * CHUNKS)


def pair_index(i, j):
    return i * (FEATURES - 1) - i * (i - 1) // 2 + j - i - 1


def kernel(**inputs):
    import numpy as np
    import concourse.bacc as bacc
    from concourse.bass_utils import run_bass_kernel_spmd

    k = np.asarray(inputs["L0_rec_kernels"])
    kg = np.zeros((D, KGROUPS, 2, D), k.dtype)
    w1 = np.asarray(inputs["W_top1"])
    w1_rows = np.zeros((ZBANKS * P, H1), w1.dtype)
    for u, (m, a) in enumerate(UNITS):
        for g in range(2):
            n = 2 * u + g
            row = (n // ZGROUPS) * P + (n % 4) * 32 + 2 * ((n % ZGROUPS) // 4)
            for half in range(2):
                i, j = 2 * a + g, 2 * m + half
                if a == m and g == 1:
                    w1_rows[row + half] = w1[j]
                elif i < j:
                    kg[:, k_groups(u)[g], half] = k[pair_index(i, j)]
                    w1_rows[row + half] = w1[FEATURES + pair_index(i, j)]
    dense_row = (ZBANKS - 1) * P + Z_LAST_ROWS
    w1_rows[dense_row:dense_row + DENSE] = w1[-DENSE:]

    ids = np.asarray(inputs["ids"]).reshape(CHUNKS, TILES, P, FEATURES).transpose(0, 2, 3, 1)
    dense = np.asarray(inputs["dense_ctx"]).reshape(CHUNKS, TILES, P, DENSE).transpose(0, 2, 1, 3)
    columns = np.concatenate([np.asarray(inputs[n]).reshape(-1, P) for n in ("b_top1", "b_top2", "W_top3")]).T
    arrays = {
        "ids": np.ascontiguousarray(ids).reshape(CHUNKS * P, FEATURES * TILES),
        "dense": np.ascontiguousarray(dense).reshape(CHUNKS * P, TILES * DENSE),
        "kg": kg.reshape(D, KGROUPS * P),
        "w1": w1_rows,
        "w2": np.asarray(inputs["W_top2"]),
        "columns": np.ascontiguousarray(columns),
    }
    for f in range(FEATURES):
        arrays[f"tbl_{f}"] = np.asarray(inputs[f"tbl_{f}"])

    nc = bacc.Bacc("TRN2", target_bir_lowering=False, num_devices=1)
    ap = {n: nc.dram_tensor(n, v.shape, mybir.dt.from_np(v.dtype), kind="ExternalInput").ap()
          for n, v in arrays.items()}
    y = nc.dram_tensor("y", (1, BATCH), F32, kind="ExternalOutput").ap()
    program(nc, ap["ids"], ap["dense"], [ap[f"tbl_{f}"] for f in range(FEATURES)], ap["kg"],
            ap["w1"], ap["w2"], ap["columns"], y)
    result = run_bass_kernel_spmd(nc, [arrays], core_ids=[0])
    return result.results[0]["y"].reshape(BATCH, 1)
```

```python
from contextlib import ExitStack

import concourse.bass as bass
from concourse import mybir

ALU = mybir.AluOpType
AXIS = mybir.AxisListType
ACT = mybir.ActivationFunctionType
F32 = mybir.dt.float32
F32R = mybir.dt.float32r
I32 = mybir.dt.int32

P = 128
FEATURES = 32
D = 64
BATCH = 2048
DENSE = 16
H1 = 512
H2 = 256
CHUNK = 512
CHUNKS = BATCH // CHUNK
TILES = CHUNK // P
ROWS = FEATURES // 2

UNITS = [(m, a) for r in range(0, ROWS, 2) for m, n in ((r, r), (r + 1, r + 2)) for a in range(n)]
NU = len(UNITS)
NB = NU // 2
LEFT = FEATURES - 1
KGROUPS = 2 * NU
KBLOCK = 4
KBLOCKS = KGROUPS // KBLOCK
KCOLS = KBLOCK * P
KSLOTS = 4
GSLOTS = 4
XSLOTS = 4
TSLOTS = 3
PSLOTS = 4
ZGROUPS = 64
ZBANKS = KGROUPS // ZGROUPS + 1
EXTRA = DENSE + FEATURES


def unit_lefts(u):
    m, a = UNITS[u]
    return (2 * (m - 1), 2 * m) if a == m else (2 * a, 2 * a + 1)


def unit_rights(u):
    m, a = UNITS[u]
    return (m - 1, m) if a == m else (m, m)


def last_unit(m):
    return UNITS.index((m | 1, m | 1))


def block_unit(b):
    return (KBLOCK * (b + 1) - 1) // 2


K_ORDER = (*range(ZBANKS - 2), ZBANKS - 1, ZBANKS - 2)
MLP_STEPS = ("h1 first", "h1 second", "h2", "y")
MLP_AT = {0: "h1 first", 2: "h1 second", 5: "h2", 8: "y"}


EXTRA_AT = NU - 8


STEPS_FIRST, STEPS_LATER = 2, 1
EAGER_FIRST, EAGER_LATER = 5, 6
K_ROUND_LEAD, K_SPLIT_LEAD = 5, 3


def chunk_order(first):
    order = []
    steps = []

    def turn(m):
        while steps and steps[0][1] < (m - 3 if steps[0][0] == "sum z" else 2 * (m - 3)):
            order.append(steps.pop(0))
        order.append(("turn", m))
        steps.extend([("sum z", m)] + [("split", f) for f in (2 * m, 2 * m + 1) if f < LEFT])
        if m < (EAGER_FIRST if first else EAGER_LATER):
            order.extend(steps)
            steps.clear()

    turn(0)
    turn(1)
    for u, (m, a) in enumerate(UNITS):
        if first:
            if m + 1 < ROWS and a == max(0, m - 3):
                turn(m + 1)
        else:
            if u in MLP_AT:
                order.append(("mlp", MLP_AT[u]))
            if u == 0:
                turn(2)
            if m + 2 < ROWS and a == 0:
                turn(m + 2)
        while any(step in steps for step in [("split", f) for f in unit_lefts(u)]):
            order.append(steps.pop(0))
        order.append(("unit", u))
        if u % 2:
            if first:
                for what, lead in (("split k", K_SPLIT_LEAD), ("round k", K_ROUND_LEAD)):
                    if KSLOTS <= (u + lead) // 2 < KBLOCKS:
                        order.append((what, (u + lead) // 2))
            for _ in range(STEPS_FIRST if first else STEPS_LATER):
                if steps:
                    order.append(steps.pop(0))
        if u % 2 == 1 and u >= 3:
            order.append(("sum", (u - 3) // 2))
        if u == EXTRA_AT:
            order += steps + [("extra", 0)]
            steps.clear()
    return order + [("sum", NB - 1)]


def psum_slots(first):
    users = [e for e in chunk_order(first) if e[0] in ("unit", "mlp")]
    return {e: (n % TSLOTS, users[n - TSLOTS] if n >= TSLOTS else None) for n, e in enumerate(users)}


K_BY_POOL = tuple(b for b in range(36, 54))


def wait_k_split(eng, k_split, k_split_by_pool, b):
    by_pool = sum(other <= b for other in K_BY_POOL)
    if b in K_BY_POOL:
        eng.wait_ge(k_split_by_pool, by_pool)
    else:
        eng.wait_ge(k_split, b + 1 - by_pool)


def wait(eng, sem, c, per_chunk, n):
    if isinstance(c, int) and c * per_chunk + n <= 0:
        return
    eng.wait_ge(sem, c * per_chunk + n)


def program(nc, ids, dense, tables, kg, w1, w2, columns, y):
    ctx = ExitStack()
    with ctx:
        def sb(name, shape, dt=F32):
            return ctx.enter_context(nc.sbuf_tensor(name, shape, dt))

        def sem(name):
            return ctx.enter_context(nc.semaphore(name))

        x_hi = sb("x_hi", [P, LEFT, CHUNK], F32R)
        x_lo = sb("x_lo", [P, LEFT, CHUNK], F32R)
        x_pair = sb("x_pair", [P, XSLOTS, CHUNK])
        x_rows = sb("x_rows", [P, GSLOTS, TILES, 2 * D])
        k_ring = sb("k_ring", [P, KSLOTS, KCOLS], F32R)
        product = sb("product", [P, PSLOTS, 2, CHUNK])
        w1_sb = sb("w1_sb", [P, ZBANKS, H1])
        w2_sb = sb("w2_sb", [P, H1 // P, H2])
        columns_sb = sb("columns_sb", [P, H1 // P + 2 * (H2 // P)])
        b1_sb, b2_sb, w3_sb = columns_sb[:, 0:4], columns_sb[:, 4:6], columns_sb[:, 6:8]
        z_sb = sb("z_sb", [P, ZBANKS, CHUNK])
        h1_sb = sb("h1_sb", [P, H1 // P, CHUNK])
        h2_sb = sb("h2_sb", [P, H2 // P, CHUNK])
        ident = sb("ident", [P, P])
        selector = sb("selector", [P, 62])
        ids_sb = sb("ids_sb", [P, FEATURES * TILES], I32)
        extra_sb = sb("extra_sb", [P, TILES, EXTRA])
        k_raw = h1_sb
        y_sb = h1_sb[0:1, 0, :]

        ps_t = ctx.enter_context(nc.psum_tensor("ps_t", [P, 2 * TSLOTS, CHUNK], F32))
        ps_z = ctx.enter_context(nc.psum_tensor("ps_z", [P, CHUNK], F32))
        ps_x = ctx.enter_context(nc.psum_tensor("ps_x", [P, CHUNK], F32))
        k_store = nc.dram_tensor("k_store", (P, KGROUPS * P), F32, kind="Internal").ap()

        weights_in = sem("weights_in")
        ones_set = sem("ones_set")
        consts_set = sem("consts_set")
        selector_set = sem("selector_set")
        ids_in = sem("ids_in")
        dense_in = sem("dense_in")
        gathered = [sem(f"gathered{s}") for s in range(GSLOTS)]
        may_gather = sem("may_gather")
        turned = sem("turned")
        hi_ready = sem("hi_ready")
        lo_ready = sem("lo_ready")
        x_ready = sem("x_ready")
        pair_ready = sem("pair_ready")
        k_raw_in = [sem(f"k_raw_in{s}") for s in range(KSLOTS)]
        k_hi_ready = sem("k_hi_ready")
        k_split = sem("k_split")
        k_split_by_pool = sem("k_split_by_pool")
        k_stored = [sem(f"k_stored{s}") for s in range(KSLOTS)]
        k_loaded = [sem(f"k_loaded{s}") for s in range(KSLOTS)]
        t_ready = sem("t_ready")
        product_ready = sem("product_ready")
        sums_done = sem("sums_done")
        z_summed = sem("z_summed")
        extra_turned = sem("extra_turned")
        extra_copied = sem("extra_copied")
        z_copied = sem("z_copied")
        h1_summed = sem("h1_summed")
        h1_ready = sem("h1_ready")
        h2_summed = sem("h2_summed")
        h2_ready = sem("h2_ready")
        y_summed = sem("y_summed")
        y_ready = sem("y_ready")
        y_stored = sem("y_stored")
        WEIGHTS = 3 * 16

        block = ctx.enter_context(nc.Block())

        @block.sync
        def _(sp):
            for b in range(KBLOCKS + 2):
                if b < KBLOCKS:
                    if b >= KSLOTS:
                        wait_k_split(sp, k_split, k_split_by_pool, b - KSLOTS)
                    for half in range(2):
                        sp.dma_start(k_raw[half * D:half * D + D, b % KSLOTS, :],
                                     kg[:, b * KCOLS:(b + 1) * KCOLS]).then_inc(k_raw_in[b % KSLOTS], 16)
                if b == 1:
                    sp.dma_start(w1_sb[:], w1.rearrange("(k p) n -> p k n", p=P)).then_inc(weights_in, 16)
                    sp.dma_start(w2_sb[:], w2.rearrange("(k p) n -> p k n", p=P)).then_inc(weights_in, 16)
                    sp.dma_start(columns_sb[:], columns).then_inc(weights_in, 16)
                if b >= 2:
                    o = b - 2
                    wait_k_split(sp, k_split, k_split_by_pool, o)
                    sp.dma_start(k_store[:, o * KCOLS:(o + 1) * KCOLS],
                                 k_ring[:, o % KSLOTS, :].bitcast(F32)).then_inc(k_stored[o % KSLOTS], 16)
            for s in range(KSLOTS):
                sp.wait_ge(k_stored[s], 16 * (KBLOCKS // KSLOTS))
            with sp.Fori(1, CHUNKS) as c:
                for b in range(KBLOCKS):
                    if b < KSLOTS:
                        wait(sp, t_ready, c - 1, NU, block_unit(KBLOCKS + b - KSLOTS) + 1)
                    else:
                        wait(sp, t_ready, c, NU, block_unit(b - KSLOTS) + 1)
                    sp.dma_start(k_ring[:, b % KSLOTS, :].bitcast(F32),
                                 k_store[:, b * KCOLS:(b + 1) * KCOLS]).then_inc(k_loaded[b % KSLOTS], 16)

        def chunk_pool(pool, c, first):
            def gather(m):
                if m >= GSLOTS:
                    wait(pool, turned, c, ROWS, m - GSLOTS + 1)
                    wait(pool, z_summed, c, ROWS, m - GSLOTS + 1)
                pool.sem_inc(may_gather, 1)
                for f in (2 * m, 2 * m + 1):
                    for t in range(TILES):
                        n = f * TILES + t
                        at = (f % 2) * D
                        nc.gpsimd.indirect_dma_start(
                            x_rows[:, m % GSLOTS, t, at:at + D], None, tables[f],
                            bass.IndirectOffsetOnAxis(ap=ids_sb[:, n:n + 1], axis=0),
                        ).then_inc(gathered[m % GSLOTS], 16)

            pool.dma_start(ids_sb[:], ids[bass.ds(c * P, P), :]).then_inc(ids_in, 16)
            wait(pool, ids_in, c, 16, 16)
            for m in range(GSLOTS):
                gather(m)
            splits = 0
            for what, n in chunk_order(first):
                if what == "sum z" and n + GSLOTS < ROWS:
                    if splits:
                        pool.wait_ge(k_split_by_pool, splits)
                    gather(n + GSLOTS)
                    m = n + GSLOTS
                elif what == "split k" and n in K_BY_POOL:
                    pool.wait_ge(gathered[m % GSLOTS], 32 * TILES * (m // GSLOTS + 1))
                    pool.wait_ge(k_hi_ready, n + 1)
                    splits += 1
                    nc.gpsimd.tensor_tensor(k_ring[D:P, n % KSLOTS, :], k_raw[D:P, n % KSLOTS, :],
                                            k_ring[D:P, n % KSLOTS, :], ALU.subtract,
                                            ).then_inc(k_split_by_pool, 1)
            if first:
                pool.wait_ge(k_split_by_pool, splits)
            wait(pool, extra_turned, c, 1, 0)
            pool.dma_start(extra_sb[:, :, 0:DENSE],
                           dense[bass.ds(c * P, P), :].rearrange("p (t k) -> p t k", k=DENSE),
                           ).then_inc(dense_in, 16)
            wait(pool, turned, c, ROWS, ROWS)
            wait(pool, z_summed, c, ROWS, ROWS)

        @block.gpsimd
        def _(pool):
            nc.gpsimd.memset(ident[:], 1.0).then_inc(ones_set, 1)
            pool.wait_ge(ones_set, 1)
            nc.gpsimd.affine_select(out=ident[:], in_=ident[:], compare_op=ALU.is_equal, fill=0.0, base=0,
                                    pattern=[[-1, P]], channel_multiplier=1).then_inc(consts_set, 1)
            pool.wait_ge(consts_set, 1)
            chunk_pool(pool, 0, True)
            with pool.Fori(1, CHUNKS) as c:
                chunk_pool(pool, c, False)

        def chunk_tensor(pe, c, first):
            slots = psum_slots(first)

            def turn(m):
                uses = ROWS // GSLOTS
                wait(pe, gathered[m % GSLOTS], c, 32 * TILES * uses, 32 * TILES * (m // GSLOTS + 1))
                wait(pe, pair_ready, c, ROWS, m)
                if m == 0:
                    wait(pe, extra_copied, c, 1, 0)
                for t in range(TILES):
                    ins = pe.transpose(ps_x[:, t * P:(t + 1) * P], x_rows[:, m % GSLOTS, t, :], ident[:])
                ins.then_inc(turned, 1)

            def slot_free(user):
                slot, before = slots[user]
                if before is None:
                    wait(pe, product_ready, c, NU, 0)
                elif before[0] == "unit":
                    wait(pe, product_ready, c, NU, before[1] + 1)
                elif before[1] == "h1 first":
                    wait(pe, h1_ready, c, H1 // P, 2 - H1 // P)
                elif before[1] == "h1 second":
                    wait(pe, h1_ready, c, H1 // P, 0)
                elif before[1] == "h2":
                    wait(pe, h2_ready, c, H2 // P, 0)
                else:
                    wait(pe, y_ready, c, 1, 0)
                return slot

            def stage1(u):
                m, a = UNITS[u]
                slot = slot_free(("unit", u))
                if a == m:
                    wait(pe, x_ready, c, LEFT, 2 * m + 1)
                elif a == m - 1:
                    wait(pe, x_ready, c, LEFT, 2 * m)
                for g, left in enumerate(unit_lefts(u)):
                    b, at = divmod(2 * u + g, KBLOCK)
                    if at == 0:
                        if first:
                            wait_k_split(pe, k_split, k_split_by_pool, b)
                        else:
                            wait(pe, k_loaded[b % KSLOTS], c - 1, 16 * (KBLOCKS // KSLOTS),
                                 16 * (b // KSLOTS + 1))
                    weights = k_ring[:, b % KSLOTS, at * P:(at + 1) * P]
                    bank = ps_t[:, 2 * slot + g, :]
                    pe.matmul(bank, weights, x_hi[:, left, :], start=True, stop=False)
                    ins = pe.matmul(bank, weights, x_lo[:, left, :], start=False, stop=True)
                ins.then_inc(t_ready, 1)

            def stage2(n):
                wait(pe, product_ready, c, NU, 2 * n + 2)
                bank, at = divmod(4 * n, ZGROUPS)
                if at == 0:
                    wait(pe, z_copied, c, ZBANKS - 1, bank)
                pair = at // 4
                for k in range(4):
                    ins = pe.matmul(ps_z[32 * k:32 * k + 32, :], selector[:, 30 - 2 * pair:62 - 2 * pair],
                                    product[:, (2 * n + k // 2) % PSLOTS, k % 2, :],
                                    start=(pair == 0), stop=(pair == ZGROUPS // 4 - 1))
                ins.then_inc(sums_done, 1)

            def turn_extra():
                wait(pe, dense_in, c, 16, 16)
                wait(pe, z_summed, c, ROWS, ROWS)
                wait(pe, pair_ready, c, ROWS, ROWS)
                for t in range(TILES):
                    ins = pe.matmul(ps_x[0:EXTRA, t * P:(t + 1) * P], extra_sb[:, t, :], ident[:],
                                    start=(t == 0), stop=(t == TILES - 1))
                ins.then_inc(extra_turned, 1)

            for what, n in chunk_order(first):
                if what == "turn":
                    turn(n)
                elif what == "unit":
                    stage1(n)
                elif what == "sum":
                    stage2(n)
                elif what == "mlp":
                    mlp_tensor(pe, c - 1, n, slot_free((what, n)))
                elif what == "extra":
                    turn_extra()

        def mlp_tensor(pe, c, step, slot):
            if step in ("h1 first", "h1 second"):
                for bank in range(2):
                    n = bank + 2 * (step == "h1 second")
                    for k in K_ORDER:
                        rows = EXTRA if k == ZBANKS - 1 else P
                        if n == 0 and k < ZBANKS - 1:
                            wait(pe, z_copied, c, ZBANKS - 1, k + 1)
                        elif n == 0:
                            wait(pe, extra_copied, c, 1, 1)
                        ins = pe.matmul(ps_t[:, 2 * slot + bank, :], w1_sb[0:rows, k, n * P:(n + 1) * P],
                                        z_sb[0:rows, k, :], start=(k == K_ORDER[0]), stop=(k == K_ORDER[-1]))
                    ins.then_inc(h1_summed, 1)
            elif step == "h2":
                for n in range(H2 // P):
                    for k in range(H1 // P):
                        if n == 0:
                            wait(pe, h1_ready, c, H1 // P, k + 1)
                        ins = pe.matmul(ps_t[:, 2 * slot + n, :], w2_sb[:, k, n * P:(n + 1) * P],
                                        h1_sb[:, k, :], start=(k == 0), stop=(k == H1 // P - 1))
                    ins.then_inc(h2_summed, 1)
            else:
                for k in range(H2 // P):
                    wait(pe, h2_ready, c, H2 // P, k + 1)
                    ins = pe.matmul(ps_t[0:1, 2 * slot, :], w3_sb[:, k:k + 1], h2_sb[:, k, :],
                                    start=(k == 0), stop=(k == H2 // P - 1))
                ins.then_inc(y_summed, 1)

        @block.tensor
        def _(pe):
            pe.wait_ge(consts_set, 1)
            pe.wait_ge(selector_set, 3)
            chunk_tensor(pe, 0, True)
            pe.wait_ge(weights_in, WEIGHTS)
            with pe.Fori(1, CHUNKS) as c:
                chunk_tensor(pe, c, False)
            pe.wait_ge(product_ready, CHUNKS * NU)
            for slot, step in enumerate(MLP_STEPS):
                if slot >= TSLOTS:
                    pe.wait_ge(h1_ready, CHUNKS * (H1 // P))
                mlp_tensor(pe, CHUNKS - 1, step, slot % TSLOTS)

        def chunk_vector(dve, c, first):
            slots = psum_slots(first)

            def sum_z(m):
                uses = ROWS // GSLOTS
                wait(dve, gathered[m % GSLOTS], c, 32 * TILES * uses, 32 * TILES * (m // GSLOTS + 1))
                if m == 0:
                    wait(dve, extra_turned, c, 1, 0)
                rows = x_rows[:, m % GSLOTS, :, :].rearrange("p t (f d) -> p t f d", d=D)
                at = DENSE + 2 * m
                dve.tensor_reduce(extra_sb[:, :, at:at + 2], rows, AXIS.X, ALU.add).then_inc(z_summed, 1)

            def split_x(f):
                lanes = slice((f % 2) * D, (f % 2) * D + D)
                wait(dve, hi_ready, c, LEFT, f + 1)
                dve.tensor_tensor(x_lo[lanes, f, :], x_pair[lanes, (f // 2) % XSLOTS, :], x_hi[lanes, f, :],
                                  ALU.subtract).then_inc(lo_ready, 1)

            def split_k(b):
                dve.wait_ge(k_hi_ready, b + 1)
                dve.tensor_tensor(k_ring[D:P, b % KSLOTS, :], k_raw[D:P, b % KSLOTS, :],
                                  k_ring[D:P, b % KSLOTS, :], ALU.subtract).then_inc(k_split, 1)

            def multiply(u):
                m, a = UNITS[u]
                wait(dve, t_ready, c, NU, u + 1)
                if a == 0:
                    wait(dve, pair_ready, c, ROWS, m + 1)
                if u >= PSLOTS:
                    wait(dve, sums_done, c, NB, (u - PSLOTS) // 2 + 1)
                elif u == 0 and not first:
                    wait(dve, sums_done, c, NB, 0)
                slot = 2 * slots[("unit", u)][0]
                if a == m:
                    right = x_pair[:, (m - 1) % XSLOTS:(m - 1) % XSLOTS + 2, :]
                else:
                    right = x_pair[:, m % XSLOTS:m % XSLOTS + 1, :].to_broadcast([P, 2, CHUNK])
                ins = dve.tensor_tensor(product[:, u % PSLOTS, :, :], ps_t[:, slot:slot + 2, :], right, ALU.mult)
                ins.then_inc(product_ready, 1)

            if first:
                for b in range(KSLOTS):
                    split_k(b)
            for what, n in chunk_order(first):
                if what == "sum z":
                    sum_z(n)
                elif what == "split":
                    split_x(n)
                elif what == "split k" and n not in K_BY_POOL:
                    split_k(n)
                elif what == "unit":
                    multiply(n)

        @block.vector
        def _(dve):
            dve.memset(selector[:], 0.0).then_inc(selector_set, 1)
            dve.wait_ge(selector_set, 1)
            dve.memset(selector[0:D, 30:31], 1.0).then_inc(selector_set, 1)
            dve.memset(selector[D:P, 31:32], 1.0).then_inc(selector_set, 1)
            chunk_vector(dve, 0, True)
            with dve.Fori(1, CHUNKS) as c:
                chunk_vector(dve, c, False)

        def chunk_scalar(act, c, first):
            slots = psum_slots(first)

            def copy_x(m):
                wait(act, turned, c, ROWS, m + 1)
                if m >= XSLOTS:
                    wait(act, product_ready, c, NU, last_unit(m - XSLOTS) + 1)
                elif m == 0 and not first:
                    wait(act, product_ready, c, NU, 0)
                pair = x_pair[:, m % XSLOTS, :]
                act.copy(pair, ps_x[:]).then_inc(pair_ready, 1)
                wait(act, pair_ready, c, ROWS, m + 1)
                features = range(2 * m, min(2 * m + 2, LEFT))
                for f in features:
                    lanes = slice((f % 2) * D, (f % 2) * D + D)
                    act.copy(x_hi[lanes, f, :], pair[lanes, :]).then_inc(hi_ready, 1)
                for f in features:
                    lanes, far = slice((f % 2) * D, (f % 2) * D + D), slice((1 - f % 2) * D, (1 - f % 2) * D + D)
                    act.copy(x_hi[far, f, :], pair[lanes, :])

            def copy_lo(f):
                lanes, far = slice((f % 2) * D, (f % 2) * D + D), slice((1 - f % 2) * D, (1 - f % 2) * D + D)
                wait(act, lo_ready, c, LEFT, f + 1)
                act.copy(x_lo[far, f, :], x_lo[lanes, f, :]).then_inc(x_ready, 1)

            def round_k(b):
                wait(act, k_raw_in[b % KSLOTS], 0, 0, 32 * (b // KSLOTS + 1))
                if b >= KSLOTS:
                    act.wait_ge(t_ready, block_unit(b - KSLOTS) + 1)
                    act.wait_ge(k_stored[b % KSLOTS], 16 * (b // KSLOTS))
                act.copy(k_ring[:, b % KSLOTS, :], k_raw[:, b % KSLOTS, :]).then_inc(k_hi_ready, 1)

            def copy_z(k):
                wait(act, sums_done, c, NB, (k + 1) * ZGROUPS // 4)
                act.copy(z_sb[:, k, :], ps_z[:]).then_inc(z_copied, 1)

            if first:
                for b in range(KSLOTS):
                    round_k(b)
            for what, n in chunk_order(first):
                if what == "turn":
                    copy_x(n)
                elif what == "split":
                    copy_lo(n)
                elif what == "round k":
                    round_k(n)
                elif what == "sum" and (n + 1) % (ZGROUPS // 4) == 0:
                    copy_z((n + 1) // (ZGROUPS // 4) - 1)
                elif what == "mlp":
                    mlp_scalar(act, c - 1, n, slots[(what, n)][0])
                elif what == "extra":
                    wait(act, extra_turned, c, 1, 1)
                    act.copy(z_sb[0:EXTRA, ZBANKS - 1, :], ps_x[0:EXTRA, :]).then_inc(extra_copied, 1)
                    if not first:
                        wait(act, y_stored, c, 16, 0)

        def mlp_scalar(act, c, step, slot):
            if step in ("h1 first", "h1 second"):
                for bank in range(2):
                    n = bank + 2 * (step == "h1 second")
                    wait(act, h1_summed, c, H1 // P, n + 1)
                    act.activation(h1_sb[:, n, :], ps_t[:, 2 * slot + bank, :], ACT.Relu,
                                   bias=b1_sb[:, n:n + 1]).then_inc(h1_ready, 1)
            elif step == "h2":
                for n in range(H2 // P):
                    wait(act, h2_summed, c, H2 // P, n + 1)
                    act.activation(h2_sb[:, n, :], ps_t[:, 2 * slot + n, :], ACT.Relu,
                                   bias=b2_sb[:, n:n + 1]).then_inc(h2_ready, 1)
            else:
                wait(act, y_summed, c, 1, 1)
                act.copy(y_sb, ps_t[0:1, 2 * slot, :]).then_inc(y_ready, 1)
                wait(act, y_ready, c, 1, 1)
                act.dma_start(y[:, bass.ds(c * CHUNK, CHUNK)], y_sb).then_inc(y_stored, 16)

        @block.scalar
        def _(act):
            chunk_scalar(act, 0, True)
            act.wait_ge(weights_in, WEIGHTS)
            with act.Fori(1, CHUNKS) as c:
                chunk_scalar(act, c, False)
            for slot, step in enumerate(MLP_STEPS):
                mlp_scalar(act, CHUNKS - 1, step, slot % TSLOTS)
            act.wait_ge(y_stored, 16 * CHUNKS)


def pair_index(i, j):
    return i * (FEATURES - 1) - i * (i - 1) // 2 + j - i - 1


def kernel(**inputs):
    import numpy as np
    import concourse.bacc as bacc
    from concourse.bass_utils import run_bass_kernel_spmd

    k = np.asarray(inputs["L0_rec_kernels"])
    kg = np.zeros((D, KGROUPS, 2, D), k.dtype)
    w1 = np.asarray(inputs["W_top1"])
    w1_rows = np.zeros((ZBANKS * P, H1), w1.dtype)
    for u in range(NU):
        for g in range(2):
            n = 2 * u + g
            row = (n // ZGROUPS) * P + (n % 4) * 32 + 2 * ((n % ZGROUPS) // 4)
            for half in range(2):
                i, j = unit_lefts(u)[g], 2 * unit_rights(u)[g] + half
                if i < j:
                    kg[:, n, half] = k[pair_index(i, j)]
                    w1_rows[row + half] = w1[FEATURES + pair_index(i, j)]
    extra = (ZBANKS - 1) * P
    w1_rows[extra:extra + DENSE] = w1[-DENSE:]
    w1_rows[extra + DENSE:extra + EXTRA] = w1[:FEATURES]

    ids = np.asarray(inputs["ids"]).reshape(CHUNKS, TILES, P, FEATURES).transpose(0, 2, 3, 1)
    dense = np.asarray(inputs["dense_ctx"]).reshape(CHUNKS, TILES, P, DENSE).transpose(0, 2, 1, 3)
    columns = np.concatenate([np.asarray(inputs[n]).reshape(-1, P) for n in ("b_top1", "b_top2", "W_top3")]).T
    arrays = {
        "ids": np.ascontiguousarray(ids).reshape(CHUNKS * P, FEATURES * TILES),
        "dense": np.ascontiguousarray(dense).reshape(CHUNKS * P, TILES * DENSE),
        "kg": kg.reshape(D, KGROUPS * P),
        "w1": w1_rows,
        "w2": np.asarray(inputs["W_top2"]),
        "columns": np.ascontiguousarray(columns),
    }
    for f in range(FEATURES):
        arrays[f"tbl_{f}"] = np.asarray(inputs[f"tbl_{f}"])

    nc = bacc.Bacc("TRN2", target_bir_lowering=False, num_devices=1)
    ap = {n: nc.dram_tensor(n, v.shape, mybir.dt.from_np(v.dtype), kind="ExternalInput").ap()
          for n, v in arrays.items()}
    y = nc.dram_tensor("y", (1, BATCH), F32, kind="ExternalOutput").ap()
    program(nc, ap["ids"], ap["dense"], [ap[f"tbl_{f}"] for f in range(FEATURES)], ap["kg"],
            ap["w1"], ap["w2"], ap["columns"], y)
    result = run_bass_kernel_spmd(nc, [arrays], core_ids=[0])
    return result.results[0]["y"].reshape(BATCH, 1)
```

```python
from contextlib import ExitStack

import concourse.bass as bass
from concourse import mybir

ALU = mybir.AluOpType
AXIS = mybir.AxisListType
ACT = mybir.ActivationFunctionType
F32 = mybir.dt.float32
F32R = mybir.dt.float32r
I32 = mybir.dt.int32

P = 128
FEATURES = 32
D = 64
BATCH = 2048
DENSE = 16
H1 = 512
H2 = 256
CHUNK = 512
CHUNKS = BATCH // CHUNK
TILES = CHUNK // P
ROWS = FEATURES // 2

UNITS = [(m, a) for r in range(0, ROWS, 2) for m, n in ((r, r), (r + 1, r + 2)) for a in range(n)]
NU = len(UNITS)
NB = NU // 2
LEFT = FEATURES - 1
KGROUPS = 2 * NU
KBLOCK = 4
KBLOCKS = KGROUPS // KBLOCK
KCOLS = KBLOCK * P
KSLOTS = 4
GSLOTS = 4
XSLOTS = 4
TSLOTS = 3
PSLOTS = 4
ZGROUPS = 64
ZBANKS = KGROUPS // ZGROUPS + 1
EXTRA = DENSE + FEATURES


def unit_lefts(u):
    m, a = UNITS[u]
    return (2 * (m - 1), 2 * m) if a == m else (2 * a, 2 * a + 1)


def unit_rights(u):
    m, a = UNITS[u]
    return (m - 1, m) if a == m else (m, m)


def last_unit(m):
    return UNITS.index((m | 1, m | 1))


def block_unit(b):
    return (KBLOCK * (b + 1) - 1) // 2


K_ORDER = (*range(ZBANKS - 2), ZBANKS - 1, ZBANKS - 2)
MLP_STEPS = ("h1 first", "h1 second", "h2", "y")
MLP_AT = {0: "h1 first", 2: "h1 second", 5: "h2", 8: "y"}
EXTRA_AT = NU - 8
STEPS_FIRST, STEPS_LATER = 2, 1
EAGER_FIRST, EAGER_LATER = 6, 4
KPAIRS = KBLOCKS // 2
RAWSLOTS = 4
TURN_LATER = {1: 1, 8: 2}
TURN_EARLY = 12
K_HEAD, K_BEHIND = [], {}
for _s in range(KPAIRS):
    for _event, _u in ((("round k", _s), 4 * _s - 9), (("split k", _s), 4 * _s - 7),
                       (("fill k", 2 * _s), 4 * _s - 5), (("fill k", 2 * _s + 1), 4 * _s - 3)):
        if _u < 0:
            K_HEAD.append(_event)
        else:
            K_BEHIND.setdefault(_u, []).append(_event)


def chunk_order(first):
    order = list(K_HEAD) if first else []
    steps = []

    def turn(m):
        while steps and steps[0][1] < (m - 3 if steps[0][0] == "sum z" else 2 * (m - 3)):
            order.append(steps.pop(0))
        order.append(("turn", m))
        steps.extend([("sum z", m)] + [("split", f) for f in (2 * m, 2 * m + 1) if f < LEFT])
        if m < (EAGER_FIRST if first else EAGER_LATER):
            order.extend(steps)
            steps.clear()

    turn(0)
    if not first:
        order.append(("last sum", NB - 1))
    turn(1)
    for u, (m, a) in enumerate(UNITS):
        if first:
            if m + 1 < ROWS and a == (max(0, m - 3) if m < TURN_EARLY else 0):
                turn(m + 1)
        else:
            if u in MLP_AT:
                order.append(("mlp", MLP_AT[u]))
            if u == 0:
                turn(2)
            if m + 2 < ROWS and u == UNITS.index((m, TURN_LATER.get(m, 0))):
                turn(m + 2)
        while any(step in steps for step in [("split", f) for f in unit_lefts(u)]):
            order.append(steps.pop(0))
        order.append(("unit", u))
        if u % 2 == 1 and u >= 3:
            order.append(("sum", (u - 3) // 2))
        if u % 2:
            if first:
                order += K_BEHIND.get(u, [])
            for _ in range(STEPS_FIRST if first else STEPS_LATER):
                if steps:
                    order.append(steps.pop(0))
        if u == EXTRA_AT:
            order += steps + [("extra", 0)]
            steps.clear()
    return order


def psum_slots(first):
    users = [e for e in chunk_order(first) if e[0] in ("unit", "mlp")]
    return {e: (n % TSLOTS, users[n - TSLOTS] if n >= TSLOTS else None) for n, e in enumerate(users)}


def wait(eng, sem, c, per_chunk, n):
    if isinstance(c, int) and c * per_chunk + n <= 0:
        return
    eng.wait_ge(sem, c * per_chunk + n)


def program(nc, ids, dense, tables, kg, w1, w2, columns, y):
    ctx = ExitStack()
    with ctx:
        def sb(name, shape, dt=F32):
            return ctx.enter_context(nc.sbuf_tensor(name, shape, dt))

        def sem(name):
            return ctx.enter_context(nc.semaphore(name))

        x_hi = sb("x_hi", [P, LEFT, CHUNK], F32R)
        x_lo = sb("x_lo", [P, LEFT, CHUNK], F32R)
        x_pair = sb("x_pair", [P, XSLOTS, CHUNK])
        x_rows = sb("x_rows", [P, GSLOTS, TILES, 2 * D])
        k_ring = sb("k_ring", [P, KSLOTS, KCOLS], F32R)
        product = sb("product", [P, PSLOTS, 2, CHUNK])
        w1_sb = sb("w1_sb", [P, ZBANKS, H1])
        w2_sb = sb("w2_sb", [P, H1 // P, H2])
        columns_sb = sb("columns_sb", [P, H1 // P + 2 * (H2 // P)])
        b1_sb, b2_sb, w3_sb = columns_sb[:, 0:4], columns_sb[:, 4:6], columns_sb[:, 6:8]
        z_sb = sb("z_sb", [P, ZBANKS, CHUNK])
        h1_sb = sb("h1_sb", [P, H1 // P, CHUNK])
        h2_sb = sb("h2_sb", [P, H2 // P, CHUNK])
        ident = sb("ident", [P, P])
        selector = sb("selector", [P, 62])
        ids_sb = sb("ids_sb", [P, FEATURES * TILES], I32)
        extra_sb = sb("extra_sb", [P, TILES, EXTRA])
        k_raw = h1_sb
        k_lo = h1_sb[:].bitcast(F32R)
        k_hi = h2_sb[:].bitcast(F32R)
        y_sb = h1_sb[0:1, 0, :]

        ps_t = ctx.enter_context(nc.psum_tensor("ps_t", [P, 2 * TSLOTS, CHUNK], F32))
        ps_z = ctx.enter_context(nc.psum_tensor("ps_z", [P, CHUNK], F32))
        ps_x = ctx.enter_context(nc.psum_tensor("ps_x", [P, CHUNK], F32))
        k_store = nc.dram_tensor("k_store", (P, KGROUPS * P), F32, kind="Internal").ap()

        weights_in = sem("weights_in")
        ones_set = sem("ones_set")
        consts_set = sem("consts_set")
        selector_set = sem("selector_set")
        ids_in = sem("ids_in")
        dense_in = sem("dense_in")
        gathered = [sem(f"gathered{s}") for s in range(GSLOTS)]
        may_gather = sem("may_gather")
        turned = sem("turned")
        hi_ready = sem("hi_ready")
        lo_ready = sem("lo_ready")
        x_ready = sem("x_ready")
        pair_ready = sem("pair_ready")
        k_raw_in = [sem(f"k_raw_in{s}") for s in range(RAWSLOTS)]
        k_hi_ready = sem("k_hi_ready")
        k_split = sem("k_split")
        k_filled = sem("k_filled")
        k_stored = [sem(f"k_stored{s}") for s in range(KSLOTS)]
        k_loaded = [sem(f"k_loaded{s}") for s in range(KSLOTS)]
        t_ready = sem("t_ready")
        product_ready = sem("product_ready")
        sums_done = sem("sums_done")
        z_summed = sem("z_summed")
        extra_turned = sem("extra_turned")
        extra_copied = sem("extra_copied")
        z_copied = sem("z_copied")
        h1_summed = sem("h1_summed")
        h1_ready = sem("h1_ready")
        h2_summed = sem("h2_summed")
        h2_ready = sem("h2_ready")
        y_summed = sem("y_summed")
        y_ready = sem("y_ready")
        y_stored = sem("y_stored")
        WEIGHTS = 3 * 16

        block = ctx.enter_context(nc.Block())

        @block.sync
        def _(sp):
            for s in range(KPAIRS + RAWSLOTS - 1):
                if s < KPAIRS:
                    if s >= RAWSLOTS:
                        sp.wait_ge(k_filled, 2 * (s - RAWSLOTS) + 2)
                    for half in range(2):
                        b = 2 * s + half
                        sp.dma_start(k_raw[half * D:half * D + D, s % RAWSLOTS, :],
                                     kg[:, b * KCOLS:(b + 1) * KCOLS]).then_inc(k_raw_in[s % RAWSLOTS], 16)
                if s == 1:
                    sp.dma_start(w1_sb[:], w1.rearrange("(k p) n -> p k n", p=P)).then_inc(weights_in, 16)
                    sp.dma_start(w2_sb[:], w2.rearrange("(k p) n -> p k n", p=P)).then_inc(weights_in, 16)
                    sp.dma_start(columns_sb[:], columns).then_inc(weights_in, 16)
                if s >= RAWSLOTS - 1:
                    for b in (2 * (s - RAWSLOTS + 1), 2 * (s - RAWSLOTS + 1) + 1):
                        sp.wait_ge(k_filled, b + 1)
                        sp.dma_start(k_store[:, b * KCOLS:(b + 1) * KCOLS],
                                     k_ring[:, b % KSLOTS, :].bitcast(F32)).then_inc(k_stored[b % KSLOTS], 16)
            for s in range(KSLOTS):
                sp.wait_ge(k_stored[s], 16 * (KBLOCKS // KSLOTS))
            with sp.Fori(1, CHUNKS) as c:
                for b in range(KBLOCKS):
                    if b < KSLOTS:
                        wait(sp, t_ready, c - 1, NU, block_unit(KBLOCKS + b - KSLOTS) + 1)
                    else:
                        wait(sp, t_ready, c, NU, block_unit(b - KSLOTS) + 1)
                    sp.dma_start(k_ring[:, b % KSLOTS, :].bitcast(F32),
                                 k_store[:, b * KCOLS:(b + 1) * KCOLS]).then_inc(k_loaded[b % KSLOTS], 16)

        def chunk_pool(pool, c):
            def gather(m):
                if m >= GSLOTS:
                    wait(pool, turned, c, ROWS, m - GSLOTS + 1)
                    wait(pool, z_summed, c, ROWS, m - GSLOTS + 1)
                pool.sem_inc(may_gather, 1)
                for f in (2 * m, 2 * m + 1):
                    for t in range(TILES):
                        n = f * TILES + t
                        at = (f % 2) * D
                        nc.gpsimd.indirect_dma_start(
                            x_rows[:, m % GSLOTS, t, at:at + D], None, tables[f],
                            bass.IndirectOffsetOnAxis(ap=ids_sb[:, n:n + 1], axis=0),
                        ).then_inc(gathered[m % GSLOTS], 16)

            pool.dma_start(ids_sb[:], ids[bass.ds(c * P, P), :]).then_inc(ids_in, 16)
            wait(pool, ids_in, c, 16, 16)
            for m in range(ROWS):
                gather(m)
            wait(pool, extra_turned, c, 1, 0)
            pool.dma_start(extra_sb[:, :, 0:DENSE],
                           dense[bass.ds(c * P, P), :].rearrange("p (t k) -> p t k", k=DENSE),
                           ).then_inc(dense_in, 16)
            wait(pool, turned, c, ROWS, ROWS)
            wait(pool, z_summed, c, ROWS, ROWS)

        @block.gpsimd
        def _(pool):
            nc.gpsimd.memset(ident[:], 1.0).then_inc(ones_set, 1)
            pool.wait_ge(ones_set, 1)
            nc.gpsimd.affine_select(out=ident[:], in_=ident[:], compare_op=ALU.is_equal, fill=0.0, base=0,
                                    pattern=[[-1, P]], channel_multiplier=1).then_inc(consts_set, 1)
            pool.wait_ge(consts_set, 1)
            chunk_pool(pool, 0)
            with pool.Fori(1, CHUNKS) as c:
                chunk_pool(pool, c)

        def stage2(pe, c, n):
            wait(pe, product_ready, c, NU, 2 * n + 2)
            bank, at = divmod(4 * n, ZGROUPS)
            if at == 0:
                wait(pe, z_copied, c, ZBANKS - 1, bank)
            pair = at // 4
            for k in range(4):
                ins = pe.matmul(ps_z[32 * k:32 * k + 32, :], selector[:, 30 - 2 * pair:62 - 2 * pair],
                                product[:, (2 * n + k // 2) % PSLOTS, k % 2, :],
                                start=(pair == 0), stop=(pair == ZGROUPS // 4 - 1))
            ins.then_inc(sums_done, 1)

        def chunk_tensor(pe, c, first):
            slots = psum_slots(first)

            def turn(m):
                uses = ROWS // GSLOTS
                wait(pe, gathered[m % GSLOTS], c, 32 * TILES * uses, 32 * TILES * (m // GSLOTS + 1))
                wait(pe, pair_ready, c, ROWS, m)
                if m == 0:
                    wait(pe, extra_copied, c, 1, 0)
                for t in range(TILES):
                    ins = pe.transpose(ps_x[:, t * P:(t + 1) * P], x_rows[:, m % GSLOTS, t, :], ident[:])
                ins.then_inc(turned, 1)

            def slot_free(user):
                slot, before = slots[user]
                if before is None:
                    wait(pe, product_ready, c, NU, 0)
                elif before[0] == "unit":
                    wait(pe, product_ready, c, NU, before[1] + 1)
                elif before[1] == "h1 first":
                    wait(pe, h1_ready, c, H1 // P, 2 - H1 // P)
                elif before[1] == "h1 second":
                    wait(pe, h1_ready, c, H1 // P, 0)
                elif before[1] == "h2":
                    wait(pe, h2_ready, c, H2 // P, 0)
                else:
                    wait(pe, y_ready, c, 1, 0)
                return slot

            def stage1(u):
                m, a = UNITS[u]
                slot = slot_free(("unit", u))
                if a == m:
                    wait(pe, x_ready, c, LEFT, 2 * m + 1)
                elif a == m - 1:
                    wait(pe, x_ready, c, LEFT, 2 * m)
                for g, left in enumerate(unit_lefts(u)):
                    b, at = divmod(2 * u + g, KBLOCK)
                    if at == 0:
                        if first:
                            pe.wait_ge(k_filled, b + 1)
                        else:
                            wait(pe, k_loaded[b % KSLOTS], c - 1, 16 * (KBLOCKS // KSLOTS),
                                 16 * (b // KSLOTS + 1))
                    weights = k_ring[:, b % KSLOTS, at * P:(at + 1) * P]
                    bank = ps_t[:, 2 * slot + g, :]
                    pe.matmul(bank, weights, x_hi[:, left, :], start=True, stop=False)
                    ins = pe.matmul(bank, weights, x_lo[:, left, :], start=False, stop=True)
                ins.then_inc(t_ready, 1)

            def turn_extra():
                wait(pe, dense_in, c, 16, 16)
                wait(pe, z_summed, c, ROWS, ROWS)
                wait(pe, pair_ready, c, ROWS, ROWS)
                for t in range(TILES):
                    ins = pe.matmul(ps_x[0:EXTRA, t * P:(t + 1) * P], extra_sb[:, t, :], ident[:],
                                    start=(t == 0), stop=(t == TILES - 1))
                ins.then_inc(extra_turned, 1)

            for what, n in chunk_order(first):
                if what == "turn":
                    turn(n)
                elif what == "unit":
                    stage1(n)
                elif what == "sum":
                    stage2(pe, c, n)
                elif what == "last sum":
                    stage2(pe, c - 1, n)
                elif what == "mlp":
                    mlp_tensor(pe, c - 1, n, slot_free((what, n)))
                elif what == "extra":
                    turn_extra()

        def mlp_tensor(pe, c, step, slot):
            if step in ("h1 first", "h1 second"):
                for bank in range(2):
                    n = bank + 2 * (step == "h1 second")
                    for k in K_ORDER:
                        rows = EXTRA if k == ZBANKS - 1 else P
                        if n == 0 and k < ZBANKS - 1:
                            wait(pe, z_copied, c, ZBANKS - 1, k + 1)
                        elif n == 0:
                            wait(pe, extra_copied, c, 1, 1)
                        ins = pe.matmul(ps_t[:, 2 * slot + bank, :], w1_sb[0:rows, k, n * P:(n + 1) * P],
                                        z_sb[0:rows, k, :], start=(k == K_ORDER[0]), stop=(k == K_ORDER[-1]))
                    ins.then_inc(h1_summed, 1)
            elif step == "h2":
                for n in range(H2 // P):
                    for k in range(H1 // P):
                        if n == 0:
                            wait(pe, h1_ready, c, H1 // P, k + 1)
                        ins = pe.matmul(ps_t[:, 2 * slot + n, :], w2_sb[:, k, n * P:(n + 1) * P],
                                        h1_sb[:, k, :], start=(k == 0), stop=(k == H1 // P - 1))
                    ins.then_inc(h2_summed, 1)
            else:
                for k in range(H2 // P):
                    wait(pe, h2_ready, c, H2 // P, k + 1)
                    ins = pe.matmul(ps_t[0:1, 2 * slot, :], w3_sb[:, k:k + 1], h2_sb[:, k, :],
                                    start=(k == 0), stop=(k == H2 // P - 1))
                ins.then_inc(y_summed, 1)

        @block.tensor
        def _(pe):
            pe.wait_ge(consts_set, 1)
            pe.wait_ge(selector_set, 3)
            chunk_tensor(pe, 0, True)
            pe.wait_ge(weights_in, WEIGHTS)
            with pe.Fori(1, CHUNKS) as c:
                chunk_tensor(pe, c, False)
            stage2(pe, CHUNKS - 1, NB - 1)
            pe.wait_ge(product_ready, CHUNKS * NU)
            for slot, step in enumerate(MLP_STEPS):
                if slot >= TSLOTS:
                    pe.wait_ge(h1_ready, CHUNKS * (H1 // P))
                mlp_tensor(pe, CHUNKS - 1, step, slot % TSLOTS)

        def chunk_vector(dve, c, first):
            slots = psum_slots(first)

            def sum_z(m):
                uses = ROWS // GSLOTS
                wait(dve, gathered[m % GSLOTS], c, 32 * TILES * uses, 32 * TILES * (m // GSLOTS + 1))
                if m == 0:
                    wait(dve, extra_turned, c, 1, 0)
                rows = x_rows[:, m % GSLOTS, :, :].rearrange("p t (f d) -> p t f d", d=D)
                at = DENSE + 2 * m
                dve.tensor_reduce(extra_sb[:, :, at:at + 2], rows, AXIS.X, ALU.add).then_inc(z_summed, 1)

            def split_x(f):
                lanes = slice((f % 2) * D, (f % 2) * D + D)
                wait(dve, hi_ready, c, LEFT, f + 1)
                dve.tensor_tensor(x_lo[lanes, f, :], x_pair[lanes, (f // 2) % XSLOTS, :], x_hi[lanes, f, :],
                                  ALU.subtract).then_inc(lo_ready, 1)

            def split_k(s):
                dve.wait_ge(k_hi_ready, s + 1)
                dve.tensor_tensor(k_lo[:, s % RAWSLOTS, :], k_raw[:, s % RAWSLOTS, :], k_hi[:, s % 2, :],
                                  ALU.subtract).then_inc(k_split, 1)

            def multiply(u):
                m, a = UNITS[u]
                wait(dve, t_ready, c, NU, u + 1)
                if a == 0:
                    wait(dve, pair_ready, c, ROWS, m + 1)
                if u >= PSLOTS:
                    wait(dve, sums_done, c, NB, (u - PSLOTS) // 2 + 1)
                elif u == 0 and not first:
                    wait(dve, sums_done, c, NB, 0)
                slot = 2 * slots[("unit", u)][0]
                if a == m:
                    right = x_pair[:, (m - 1) % XSLOTS:(m - 1) % XSLOTS + 2, :]
                else:
                    right = x_pair[:, m % XSLOTS:m % XSLOTS + 1, :].to_broadcast([P, 2, CHUNK])
                ins = dve.tensor_tensor(product[:, u % PSLOTS, :, :], ps_t[:, slot:slot + 2, :], right, ALU.mult)
                ins.then_inc(product_ready, 1)

            for what, n in chunk_order(first):
                if what == "sum z":
                    sum_z(n)
                elif what == "split":
                    split_x(n)
                elif what == "split k":
                    split_k(n)
                elif what == "unit":
                    multiply(n)

        @block.vector
        def _(dve):
            dve.memset(selector[:], 0.0).then_inc(selector_set, 1)
            dve.wait_ge(selector_set, 1)
            dve.memset(selector[0:D, 30:31], 1.0).then_inc(selector_set, 1)
            dve.memset(selector[D:P, 31:32], 1.0).then_inc(selector_set, 1)
            chunk_vector(dve, 0, True)
            with dve.Fori(1, CHUNKS) as c:
                chunk_vector(dve, c, False)

        def copy_z(act, c, k):
            wait(act, sums_done, c, NB, (k + 1) * ZGROUPS // 4)
            act.copy(z_sb[:, k, :], ps_z[:]).then_inc(z_copied, 1)

        def chunk_scalar(act, c, first):
            slots = psum_slots(first)

            def copy_x(m):
                wait(act, turned, c, ROWS, m + 1)
                if m >= XSLOTS:
                    wait(act, product_ready, c, NU, last_unit(m - XSLOTS) + 1)
                elif m == 0 and not first:
                    wait(act, product_ready, c, NU, 0)
                pair = x_pair[:, m % XSLOTS, :]
                act.copy(pair, ps_x[:]).then_inc(pair_ready, 1)
                wait(act, pair_ready, c, ROWS, m + 1)
                features = range(2 * m, min(2 * m + 2, LEFT))
                for f in features:
                    lanes = slice((f % 2) * D, (f % 2) * D + D)
                    act.copy(x_hi[lanes, f, :], pair[lanes, :]).then_inc(hi_ready, 1)
                for f in features:
                    lanes, far = slice((f % 2) * D, (f % 2) * D + D), slice((1 - f % 2) * D, (1 - f % 2) * D + D)
                    act.copy(x_hi[far, f, :], pair[lanes, :])

            def copy_lo(f):
                lanes, far = slice((f % 2) * D, (f % 2) * D + D), slice((1 - f % 2) * D, (1 - f % 2) * D + D)
                wait(act, lo_ready, c, LEFT, f + 1)
                act.copy(x_lo[far, f, :], x_lo[lanes, f, :]).then_inc(x_ready, 1)

            def round_k(s):
                act.wait_ge(k_raw_in[s % RAWSLOTS], 32 * (s // RAWSLOTS + 1))
                if s >= 2:
                    act.wait_ge(k_filled, 2 * s - 2)
                act.copy(k_hi[:, s % 2, :], k_raw[:, s % RAWSLOTS, :]).then_inc(k_hi_ready, 1)

            def fill_k(b):
                s, half = divmod(b, 2)
                act.wait_ge(k_split, s + 1)
                if b >= KSLOTS:
                    act.wait_ge(t_ready, block_unit(b - KSLOTS) + 1)
                    act.wait_ge(k_stored[b % KSLOTS], 16 * (b // KSLOTS))
                near, far = slice(half * D, half * D + D), slice(D - half * D, P - half * D)
                act.copy(k_ring[near, b % KSLOTS, :], k_hi[near, s % 2, :])
                act.copy(k_ring[far, b % KSLOTS, :], k_lo[near, s % RAWSLOTS, :]).then_inc(k_filled, 1)

            for what, n in chunk_order(first):
                if what == "turn":
                    copy_x(n)
                elif what == "split":
                    copy_lo(n)
                elif what == "round k":
                    round_k(n)
                elif what == "fill k":
                    fill_k(n)
                elif what == "sum" and (n + 1) % (ZGROUPS // 4) == 0:
                    copy_z(act, c, (n + 1) // (ZGROUPS // 4) - 1)
                elif what == "last sum":
                    copy_z(act, c - 1, ZBANKS - 2)
                elif what == "mlp":
                    mlp_scalar(act, c - 1, n, slots[(what, n)][0])
                elif what == "extra":
                    wait(act, extra_turned, c, 1, 1)
                    act.copy(z_sb[0:EXTRA, ZBANKS - 1, :], ps_x[0:EXTRA, :]).then_inc(extra_copied, 1)
                    if not first:
                        wait(act, y_stored, c, 16, 0)

        def mlp_scalar(act, c, step, slot):
            if step in ("h1 first", "h1 second"):
                for bank in range(2):
                    n = bank + 2 * (step == "h1 second")
                    wait(act, h1_summed, c, H1 // P, n + 1)
                    act.activation(h1_sb[:, n, :], ps_t[:, 2 * slot + bank, :], ACT.Relu,
                                   bias=b1_sb[:, n:n + 1]).then_inc(h1_ready, 1)
            elif step == "h2":
                for n in range(H2 // P):
                    wait(act, h2_summed, c, H2 // P, n + 1)
                    act.activation(h2_sb[:, n, :], ps_t[:, 2 * slot + n, :], ACT.Relu,
                                   bias=b2_sb[:, n:n + 1]).then_inc(h2_ready, 1)
            else:
                wait(act, y_summed, c, 1, 1)
                act.copy(y_sb, ps_t[0:1, 2 * slot, :]).then_inc(y_ready, 1)
                wait(act, y_ready, c, 1, 1)
                act.dma_start(y[:, bass.ds(c * CHUNK, CHUNK)], y_sb).then_inc(y_stored, 16)

        @block.scalar
        def _(act):
            chunk_scalar(act, 0, True)
            act.wait_ge(weights_in, WEIGHTS)
            with act.Fori(1, CHUNKS) as c:
                chunk_scalar(act, c, False)
            copy_z(act, CHUNKS - 1, ZBANKS - 2)
            for slot, step in enumerate(MLP_STEPS):
                mlp_scalar(act, CHUNKS - 1, step, slot % TSLOTS)
            act.wait_ge(y_stored, 16 * CHUNKS)


def pair_index(i, j):
    return i * (FEATURES - 1) - i * (i - 1) // 2 + j - i - 1


def kernel(**inputs):
    import numpy as np
    import concourse.bacc as bacc
    from concourse.bass_utils import run_bass_kernel_spmd

    k = np.asarray(inputs["L0_rec_kernels"])
    kg = np.zeros((D, KGROUPS, 2, D), k.dtype)
    w1 = np.asarray(inputs["W_top1"])
    w1_rows = np.zeros((ZBANKS * P, H1), w1.dtype)
    for u in range(NU):
        for g in range(2):
            n = 2 * u + g
            row = (n // ZGROUPS) * P + (n % 4) * 32 + 2 * ((n % ZGROUPS) // 4)
            for half in range(2):
                i, j = unit_lefts(u)[g], 2 * unit_rights(u)[g] + half
                if i < j:
                    kg[:, n, half] = k[pair_index(i, j)]
                    w1_rows[row + half] = w1[FEATURES + pair_index(i, j)]
    extra = (ZBANKS - 1) * P
    w1_rows[extra:extra + DENSE] = w1[-DENSE:]
    w1_rows[extra + DENSE:extra + EXTRA] = w1[:FEATURES]

    ids = np.asarray(inputs["ids"]).reshape(CHUNKS, TILES, P, FEATURES).transpose(0, 2, 3, 1)
    dense = np.asarray(inputs["dense_ctx"]).reshape(CHUNKS, TILES, P, DENSE).transpose(0, 2, 1, 3)
    columns = np.concatenate([np.asarray(inputs[n]).reshape(-1, P) for n in ("b_top1", "b_top2", "W_top3")]).T
    arrays = {
        "ids": np.ascontiguousarray(ids).reshape(CHUNKS * P, FEATURES * TILES),
        "dense": np.ascontiguousarray(dense).reshape(CHUNKS * P, TILES * DENSE),
        "kg": kg.reshape(D, KGROUPS * P),
        "w1": w1_rows,
        "w2": np.asarray(inputs["W_top2"]),
        "columns": np.ascontiguousarray(columns),
    }
    for f in range(FEATURES):
        arrays[f"tbl_{f}"] = np.asarray(inputs[f"tbl_{f}"])

    nc = bacc.Bacc("TRN2", target_bir_lowering=False, num_devices=1)
    ap = {n: nc.dram_tensor(n, v.shape, mybir.dt.from_np(v.dtype), kind="ExternalInput").ap()
          for n, v in arrays.items()}
    y = nc.dram_tensor("y", (1, BATCH), F32, kind="ExternalOutput").ap()
    program(nc, ap["ids"], ap["dense"], [ap[f"tbl_{f}"] for f in range(FEATURES)], ap["kg"],
            ap["w1"], ap["w2"], ap["columns"], y)
    result = run_bass_kernel_spmd(nc, [arrays], core_ids=[0])
    return result.results[0]["y"].reshape(BATCH, 1)
```
